# Optimizing a Trainium2 kernel written in Bass

```python
import numpy as np
import jax
import jax.numpy as jnp

def _softmax(x, axis=-1):
    return jax.nn.softmax(x, axis=axis)

def _gelu(x):
    return jax.nn.gelu(x, approximate=True)

def _silu(x):
    return jax.nn.silu(x)

def _sigmoid(x):
    return jax.nn.sigmoid(x)

def _layernorm(x, axis=-1, eps=1e-05):
    m = jnp.mean(x, axis=axis, keepdims=True)
    v = jnp.var(x, axis=axis, keepdims=True)
    return (x - m) / jnp.sqrt(v + eps)

def _scatter_add(tgt, idx, src, axis=0):
    return tgt.at[idx].add(src)

def _segment_sum(src, seg, n):
    return jax.ops.segment_sum(src, seg, n)
kernel_name = 'mk_gnn_ffn_d1_gnn_r32_635c2d'

def setup_inputs(seed: int=0):
    np.random.seed(seed)
    _w = jnp.asarray

    def _rec_inputs():
        import jax
        import jax.numpy as jnp
        _gk = jax.random.key(seed)
        x = -8.776e-05 + 1 * jax.random.normal(jax.random.fold_in(_gk, 1), (10000, 512), jnp.float32)
        src = jax.random.randint(jax.random.fold_in(_gk, 2), (5000,), 0, 10000, jnp.int32)
        dst = jax.random.randint(jax.random.fold_in(_gk, 3), (5000,), 0, 10000, jnp.int32)
        _o = jnp.argsort(dst, stable=True)
        src = src[_o]
        dst = dst[_o]
        edge_type_2 = jax.random.randint(jax.random.fold_in(_gk, 12), (5000,), 0, 2, jnp.int32)
        return (x, src, dst, edge_type_2)
    x, src, dst, edge_type_2 = _rec_inputs()

    def _L0_gnn_setup():
        import jax, jax.numpy as jnp
        import numpy as np
        NUM_RELATIONS = 2
        NUM_BASES = 30
        HIDDEN = 512
        N_NODES = 10000
        N_EDGES = 5000

        def rgcn_gate_layer(x, row, col, edge_type, basis, att, gate_w, root, bias):
            H = x.shape[1]
            w = jnp.einsum('rb,bio->rio', att, basis)
            x_j = x[col]
            msgs = []
            for r in range(NUM_RELATIONS):
                gate = jax.nn.sigmoid(x_j @ gate_w[r, :, 0])
                msgs.append(gate[:, None] * x_j @ w[r])
            msg = jnp.where((edge_type == 0)[:, None], msgs[0], msgs[1])
            agg = jax.ops.segment_sum(msg, row, num_segments=x.shape[0])
            return agg + x @ root + bias
        key = jax.random.key(seed)
        ks = jax.random.split(key, 16)
        H, R, B = (HIDDEN, NUM_RELATIONS, NUM_BASES)
        bound = 1.0 / np.sqrt(B * H)
        u = lambda k, shape: jax.random.uniform(k, shape, jnp.float32, -bound, bound)
        inp = {'x': jax.random.normal(ks[0], (N_NODES, H), jnp.float32), 'edge_index': jax.random.randint(ks[1], (2, N_EDGES), 0, N_NODES, jnp.int32), 'edge_type': jax.random.randint(ks[2], (N_EDGES,), 0, R, jnp.int32), 'basis1': u(ks[3], (B, H, H)), 'att1': u(ks[4], (R, B)), 'gate_w1': u(ks[5], (R, H, 1)), 'root1': u(ks[6], (H, H)), 'bias1': u(ks[7], (H,)), 'basis2': u(ks[8], (B, H, H)), 'att2': u(ks[9], (R, B)), 'gate_w2': u(ks[10], (R, H, 1)), 'root2': u(ks[11], (H, H)), 'bias2': u(ks[12], (H,))}
        return inp
    _L0_gnn_all = _L0_gnn_setup()
    _L0_gnn_in = {k: v for k, v in _L0_gnn_all.items() if k in ('basis1', 'att1', 'gate_w1', 'root1', 'bias1', 'basis2', 'att2', 'gate_w2', 'root2', 'bias2')}
    del _L0_gnn_all

    def _L0_ffn_setup():
        import jax, jax.numpy as jnp
        import numpy as np
        B, S, D, F, E, NS, K = (2, 64, 512, 64, 8, 2, 2)
        key = jax.random.key(seed)
        ks = jax.random.split(key, 6)
        scale = 0.02

        def p(k, shape):
            return jax.random.normal(k, shape, jnp.float32) * scale
        return {'x': jax.random.normal(ks[0], (B, S, D), jnp.float32), 'gate_w': p(ks[1], (E, D)), 'gate_b': jnp.zeros((E,), jnp.float32), 'sw1': p(ks[2], (NS, F, D)), 'sb1': jnp.zeros((NS, F), jnp.float32), 'sw2': p(ks[3], (NS, D, F)), 'sb2': jnp.zeros((NS, D), jnp.float32), 'rw1': p(ks[4], (E, F, D)), 'rb1': jnp.zeros((E, F), jnp.float32), 'rw2': p(ks[5], (E, D, F)), 'rb2': jnp.zeros((E, D), jnp.float32)}
    _L0_ffn_all = _L0_ffn_setup()
    _L0_ffn_in = {k: v for k, v in _L0_ffn_all.items() if k in ('gate_w', 'gate_b', 'sw1', 'sb1', 'sw2', 'sb2', 'rw1', 'rb1', 'rw2', 'rb2')}
    del _L0_ffn_all
    return {'x': x, 'src': src, 'dst': dst, 'edge_type_2': edge_type_2, 'L0_gnn_basis1': _L0_gnn_in['basis1'], 'L0_gnn_att1': _L0_gnn_in['att1'], 'L0_gnn_gate_w1': _L0_gnn_in['gate_w1'], 'L0_gnn_root1': _L0_gnn_in['root1'], 'L0_gnn_bias1': _L0_gnn_in['bias1'], 'L0_gnn_basis2': _L0_gnn_in['basis2'], 'L0_gnn_att2': _L0_gnn_in['att2'], 'L0_gnn_gate_w2': _L0_gnn_in['gate_w2'], 'L0_gnn_root2': _L0_gnn_in['root2'], 'L0_gnn_bias2': _L0_gnn_in['bias2'], 'L0_ffn_gate_w': _L0_ffn_in['gate_w'], 'L0_ffn_gate_b': _L0_ffn_in['gate_b'], 'L0_ffn_sw1': _L0_ffn_in['sw1'], 'L0_ffn_sb1': _L0_ffn_in['sb1'], 'L0_ffn_sw2': _L0_ffn_in['sw2'], 'L0_ffn_sb2': _L0_ffn_in['sb2'], 'L0_ffn_rw1': _L0_ffn_in['rw1'], 'L0_ffn_rb1': _L0_ffn_in['rb1'], 'L0_ffn_rw2': _L0_ffn_in['rw2'], 'L0_ffn_rb2': _L0_ffn_in['rb2']}

def reference(x, src, dst, edge_type_2, L0_gnn_basis1, L0_gnn_att1, L0_gnn_gate_w1, L0_gnn_root1, L0_gnn_bias1, L0_gnn_basis2, L0_gnn_att2, L0_gnn_gate_w2, L0_gnn_root2, L0_gnn_bias2, L0_ffn_gate_w, L0_ffn_gate_b, L0_ffn_sw1, L0_ffn_sb1, L0_ffn_sw2, L0_ffn_sb2, L0_ffn_rw1, L0_ffn_rb1, L0_ffn_rw2, L0_ffn_rb2):
    import jax
    import jax.numpy as jnp

    def _L0_gnn_ref(x, edge_index, edge_type, basis1, att1, gate_w1, root1, bias1, basis2, att2, gate_w2, root2, bias2):
        import jax, jax.numpy as jnp
        import numpy as np
        NUM_RELATIONS = 2
        NUM_BASES = 30
        HIDDEN = 512
        N_NODES = 10000
        N_EDGES = 5000

        def rgcn_gate_layer(x, row, col, edge_type, basis, att, gate_w, root, bias):
            H = x.shape[1]
            w = jnp.einsum('rb,bio->rio', att, basis)
            x_j = x[col]
            msgs = []
            for r in range(NUM_RELATIONS):
                gate = jax.nn.sigmoid(x_j @ gate_w[r, :, 0])
                msgs.append(gate[:, None] * x_j @ w[r])
            msg = jnp.where((edge_type == 0)[:, None], msgs[0], msgs[1])
            agg = jax.ops.segment_sum(msg, row, num_segments=x.shape[0])
            return agg + x @ root + bias
        row, col = (edge_index[0], edge_index[1])
        h = jax.nn.relu(rgcn_gate_layer(x, row, col, edge_type, basis1, att1, gate_w1, root1, bias1))
        out = rgcn_gate_layer(h, row, col, edge_type, basis2, att2, gate_w2, root2, bias2)
        return out

    def _L0_ffn_ref(x, gate_w, gate_b, sw1, sb1, sw2, sb2, rw1, rb1, rw2, rb2):
        import jax, jax.numpy as jnp
        import numpy as np
        B, S, D, F, E, NS, K = (2, 64, 512, 64, 8, 2, 2)
        b, s, d = x.shape
        t = x.reshape(-1, d)
        T = t.shape[0]
        hs = jax.nn.gelu(jnp.einsum('td,nfd->ntf', t, sw1) + sb1[:, None, :], approximate=False)
        shared = jnp.einsum('ntf,ndf->td', hs, sw2) + sb2.sum(axis=0)
        logits = t @ gate_w.T + gate_b
        probs = jax.nn.softmax(logits, axis=-1)
        top_v, top_i = jax.lax.top_k(probs, K)
        cw = jnp.zeros_like(probs).at[jnp.arange(T)[:, None], top_i].add(top_v)
        hr = jax.nn.gelu(jnp.einsum('td,efd->etf', t, rw1) + rb1[:, None, :], approximate=False)
        oe = jnp.einsum('etf,edf->etd', hr, rw2) + rb2[:, None, :]
        routed = jnp.einsum('etd,te->td', oe, cw)
        return (shared + routed).reshape(b, s, d)
    edge_index = jnp.stack([src, dst])
    x = x + _L0_gnn_ref(_layernorm(x, axis=-1), edge_index, edge_type_2, L0_gnn_basis1, L0_gnn_att1, L0_gnn_gate_w1, L0_gnn_root1, L0_gnn_bias1, L0_gnn_basis2, L0_gnn_att2, L0_gnn_gate_w2, L0_gnn_root2, L0_gnn_bias2)
    x = x + _L0_ffn_ref(_layernorm(x, axis=-1)[None], L0_ffn_gate_w, L0_ffn_gate_b, L0_ffn_sw1, L0_ffn_sb1, L0_ffn_sw2, L0_ffn_sb2, L0_ffn_rw1, L0_ffn_rb1, L0_ffn_rw2, L0_ffn_rb2)[0]
    return x

_drawn_inputs = setup_inputs


def setup_inputs(seed=0):
    import zlib

    import numpy as np

    out = dict(_drawn_inputs(seed))
    spreads = {'L0_ffn_gate_b': (0.0, 0.59),
     'L0_ffn_sb1': (0.0, 0.676),
     'L0_ffn_sb2': (0.0, 0.1),
     'L0_ffn_rb1': (0.0, 0.8),
     'L0_ffn_rb2': (0.0, 0.281)}
    factors = {'L0_gnn_basis1': 8.0,
     'L0_gnn_att1': 8.0,
     'L0_gnn_gate_w1': 26.628,
     'L0_gnn_root1': 8.0,
     'L0_gnn_bias1': 8.0,
     'L0_gnn_basis2': 8.0,
     'L0_gnn_att2': 8.0,
     'L0_gnn_gate_w2': 38.203,
     'L0_gnn_root2': 7.123,
     'L0_gnn_bias2': 8.0,
     'L0_ffn_rw1': 4.964,
     'L0_ffn_rw2': 4.666}
    for name, (base, spread) in spreads.items():
        noise = np.random.default_rng([zlib.crc32(name.encode()), seed]).standard_normal(out[name].shape)
        drawn = base * np.exp(spread * noise) if base else spread * noise
        out[name] = jnp.asarray(drawn.astype(out[name].dtype))
    for name, factor in factors.items():
        out[name] = (out[name] * factor).astype(out[name].dtype)
    return out
```

```python
from contextlib import ExitStack

import concourse.bass as bass
from concourse import mybir

F32 = mybir.dt.float32
F32R = mybir.dt.float32r
I32 = mybir.dt.int32
ALU = mybir.AluOpType
ACT = mybir.ActivationFunctionType
AX_X = mybir.AxisListType.X

P = 128
EPS = 1e-5


class Pos:

    def __init__(self, k, i=None, step=0):
        self.k, self.i, self.step = k, i, step

    def __add__(self, n):
        return Pos(self.k + n, self.i, self.step)

    def times(self, a, b=0):
        c = a * self.k + b
        return c if self.i is None else self.i * (a * self.step) + c

    def div(self, n):
        assert self.step % n == 0
        return Pos(self.k // n, self.i, self.step // n)

    def mod(self, n):
        assert self.step % n == 0
        return self.k % n


def wait(eng, sem, value):
    if not isinstance(value, int) or value > 0:
        eng.wait_ge(sem, value)


def gnn_moe_kernel(nc, x, src, dst, etype, basis, att, gate_w, root, bias,
                   moe_gate_wT, moe_gate_b, w1T, sb1, rb1, w2T, sb2, rb2, out):
    N, H = x.shape
    E = src.shape[0]
    KC = H // P
    NB = basis[0].shape[0]
    R = att[0].shape[0]
    NE = rb1.shape[0]
    FH = w1T.shape[1]
    FC = FH // P
    NT = N // P + 1
    TAIL = N - P
    NG = NT // 2
    assert N % P and NT == 2 * NG + 1 and NT % 8 == 7
    ET = (E + R * (P - 1)) // P
    assert ET % 4 == 1
    ER, EC = 125, E // 125
    ISUB = 120 // NB
    BP = NB * ISUB
    CS = P // 4
    TRASH = N
    NQ = N // (4 * P) + 1
    QT = 4
    QLAST = 3
    A0, B0, C0, D0 = 0, NT, NT + ET, 2 * NT + ET
    SA, SB, SC, SD = "A", "B", "C", "D"

    y1 = nc.dram_tensor("y1", (N + P, H), F32, kind="Internal").ap()
    z = nc.dram_tensor("z", (N + P, H), F32, kind="Internal").ap()
    records = nc.dram_tensor("records", (P * ET, 2), I32, kind="Internal").ap()
    src_rows = nc.dram_tensor("src_rows", (ET, P), F32, kind="Internal").ap()
    w_dram = [nc.dram_tensor(f"w_dram{l}", (R * ISUB, P, H), F32, kind="Internal").ap() for l in range(2)]

    ctx = ExitStack()
    with ctx:
        base = nc.sbuf_base + (-nc.sbuf_base) % 64
        top = [base]

        def place(name, shape, dt=F32, at=None):
            size = 4
            for n in shape[1:]:
                size *= n
            if at is None:
                at = top[0]
                top[0] = at + size + (-size) % 32
            return nc.alloc_sbuf_tensor_at(name, shape, dt, offset=at), at + size + (-size) % 32

        def sb(name, shape, dt=F32):
            return place(name, shape, dt)[0]

        ident = sb("ident", [P, P])
        lower = sb("lower", [P, P])
        before = sb("before", [P, P])
        ones = sb("ones", [P, P])
        gatew = [sb(f"gatew{l}", [P, R, H]) for l in range(2)]
        bias_b = [sb(f"bias_b{l}", [P, H]) for l in range(2)]
        att_c = sb("att_c", [BP, 2, R])
        sub_mask = sb("sub_mask", [BP, ISUB])
        att_block = [sb(f"att_block{l}", [BP, 32]) for l in range(2)]
        rel = sb("rel", [P, ET + 1], I32)
        dst_slot = sb("dst_slot", [P, ET], I32)
        src_slot = sb("src_slot", [P, ET])
        scat_slot = sb("scat_slot", [P, ET], I32)
        dups = sb("dups", [P, ET])
        trash_f = sb("trash_f", [P, 1])
        keep = sb("keep", [P, ET])
        gidx = sb("gidx", [P, 4], I32)
        sidx = sb("sidx", [P, 2], I32)
        bn = sb("bn", [P, 4, 2, 6])
        mv = sb("mv", [P, 4, 2, 2])
        rstd = sb("rstd", [P, 4, 2])
        nmr = sb("nmr", [P, 4, 2])
        ebn = sb("ebn", [P, 4, 6])
        emv = sb("emv", [P, 4, 2])
        erstd = sb("erstd", [P, 4, 1])
        enmr = sb("enmr", [P, 4, 1])
        logit = sb("logit", [P, 4])
        gate = sb("gate", [P, 4])
        e_type = sb("e_type", [ER, EC], I32)
        e_src = sb("e_src", [ER, EC], I32)
        e_dst = sb("e_dst", [ER, EC], I32)
        e_rec = sb("e_rec", [ER, EC, 2], I32)
        e_zero = sb("e_zero", [ER, EC])
        e_scan = sb("e_scan", [ER, EC])
        e_f = sb("e_f", [ER, 4, EC])
        e_i = sb("e_i", [ER, 4, EC], I32)
        e_pos = sb("e_pos", [ER, EC], I32)
        e_iota = sb("e_iota", [ER, EC])
        r_pos = sb("r_pos", [ER, 2], I32)
        r_rec = sb("r_rec", [ER, 2, 2], I32)
        n_col = sb("n_col", [P, 4], I32)
        minus_half = sb("minus_half", [P, 4])
        n_colf = sb("n_colf", [P, 4])
        t_iota = sb("t_iota", [P, ET + 1])
        fill_rec = sb("fill_rec", [P, ET, 2], I32)
        zeros = sb("zeros", [P, H])
        gw = sb("gw", [P, KC, NE])
        gwh = sb("gwh", [P, KC, NE], F32R)
        gwl = sb("gwl", [P, KC, NE], F32R)
        gbias = sb("gbias", [P, NE])
        b1 = sb("b1", [P, FC])
        NR2 = NE + 2
        sel = sb("sel", [3 * NR2, NE, 64], F32R)
        b2 = sb("b2", [3 * NR2, H])
        b2lo = sb("b2lo", [3 * NR2, H])
        b2r = sb("b2r", [3 * NR2, H], F32R)
        lo_row = sb("lo_row", [3 * NR2, 1])

        common = top[0]
        w1h, e1 = place("w1h", [P, KC, FH], F32R, at=common)
        w1l, e2 = place("w1l", [P, KC, FH], F32R, at=e1)
        w2h, e3 = place("w2h", [P, FC, H], F32R, at=e2)
        w2l, e4 = place("w2l", [P, FC, H], F32R, at=e3)
        root1h, a1 = place("root1h", [P, KC, H], F32R, at=common)
        root1l, a2 = place("root1l", [P, KC, H], F32R, at=a1)
        basis_t, a3 = place("basis_t", [BP, 2, 4, H], at=a2)
        wevac, a4 = place("wevac", [P, 2, 2, H], at=a3)
        late = max(e4, a4)
        top[0] = late
        root2h, root2l = sb("root2h", [P, KC, H], F32R), sb("root2l", [P, KC, H], F32R)
        wrh, wrl = sb("wrh", [P, R * ISUB, H], F32R), sb("wrl", [P, R * ISUB, H], F32R)
        m_at = top[0]
        same = sb("same", [P, ET, P], F32R)
        stage0, s1 = place("stage0", [P, KC, H], at=m_at)
        stage1, s2 = place("stage1", [P, KC, H], at=s1)
        assert s2 <= top[0]
        xy_at = top[0]
        xin = sb("xin", [P, 4, 2, H])
        yout = sb("yout", [P, 2, 2, H])
        stage_w1, s3 = place("stage_w1", [P, KC, FH], at=xy_at)
        stage_w2, s4 = place("stage_w2", [P, FC, H], at=s3)
        assert s4 <= top[0]
        xn_a = sb("xn_a", [P, 2, H])
        th, tl = sb("th", [P, 2, H], F32R), sb("tl", [P, 2, H], F32R)
        gx = sb("gx", [P, 4, H])
        xn_e = sb("xn_e", [P, 4, H])
        eh, el = sb("eh", [P, 2, H], F32R), sb("el", [P, 2, H], F32R)
        msg = sb("msg", [P, 2, H])
        scratch = sb("scratch", [P, H])
        assert top[0] <= nc.sbuf_usable_end, (top[0], nc.sbuf_usable_end)
        top[0] = late
        zr = sb("zr", [P, 4, QT, H])
        xr = sb("xr", [P, 2, QT, H])
        tn = sb("tn", [P, QT, H])
        tth, ttl = sb("tth", [P, 2, KC, QT * P], F32R), sb("ttl", [P, 2, KC, QT * P], F32R)
        gel = sb("gel", [P, 2, QT * P])
        gsc = sb("gsc", [P, 2, QT * P])
        gth, gtl = sb("gth", [P, FC, QT * P], F32R), sb("gtl", [P, FC, QT * P], F32R)
        cwt = sb("cwt", [3 * NR2, 2, QT * P], F32R)
        qbn = sb("qbn", [P, 2, QT, 6])
        qmv = sb("qmv", [P, 2, QT, 2])
        qrstd = sb("qrstd", [P, 2, QT])
        qnmr = sb("qnmr", [P, 2, QT])
        lg = sb("lg", [P, QT, NE])
        lg2 = sb("lg2", [P, QT, NE])
        mx = sb("mx", [P, QT])
        ex = sb("ex", [P, QT, NE])
        sm = sb("sm", [P, QT])
        rc = sb("rc", [P, QT])
        pr = sb("pr", [P, QT, NE])
        mx8 = sb("mx8", [P, QT, 8])
        topv = sb("topv", [P, QT, 8])
        rest = sb("rest", [P, QT, NE])
        cw = sb("cw", [P, QT, NE])
        cwh = sb("cwh", [P, QT, NE], F32R)
        cw3 = sb("cw3", [P, QT, 3, NR2])
        assert top[0] <= nc.sbuf_usable_end, (top[0], nc.sbuf_usable_end)

        bank = [ctx.enter_context(nc.psum_tensor(f"bank{i}", [P, 512], F32)) for i in range(8)]
        tpb, outb, wb, cnt = bank[0:2], bank[2:4], bank[4:6], bank[6]

        def sem(name):
            return ctx.enter_context(nc.semaphore(name))

        s_edges = sem("edges_loaded")
        s_small = sem("small_loaded")
        s_root = [sem("root1_loaded"), sem("root2_loaded")]
        s_pool = sem("pool_consts")
        s_const = sem("consts_made")
        s_apart = [sem("vector_waited"), sem("gpsimd_waited")]
        s_zero_rows = sem("trash_rows_zeroed")
        s_chain = sem("vector_chain")
        s_rooth = sem("root_hi")
        s_rootl = sem("root_lo")
        s_cnt = sem("relation_counted")
        s_pos = sem("positions_known")
        s_fill = sem("records_filled")
        s_rec = sem("record_scattered")
        s_recl = sem("records_loaded")
        s_slots = sem("slots_unpacked")
        s_srow = sem("src_rows_stored")
        s_srcb = sem("src_rows_broadcast")
        s_same = sem("same_known")
        s_sidx = sem("scatter_rows_known")
        s_xin = [sem(f"tile_pair_loaded{i}") for i in range(4)]
        s_stat = sem("stats_known")
        s_norm = sem("tile_normalised")
        s_tp = sem("transposed")
        s_hi = sem("hi_written")
        s_lo = sem("lo_written")
        s_mm = sem("product_done")
        s_y = sem("y_written")
        s_msg = sem("message_written")
        s_ystore = [sem(f"y_stored{i}") for i in range(2)]
        s_gx = [sem(f"gathered{i}") for i in range(4)]
        s_gi = sem("gather_index")
        s_si = sem("scatter_index")
        s_est = sem("edge_stats_known")
        s_xn = sem("edge_rows_normalised")
        s_gate = sem("gate_logit")
        s_sig = sem("gate_value")
        s_eh = sem("gated_hi")
        s_el = sem("gated_lo")
        s_scat = sem("scattered")
        s_bin = [sem(f"basis_loaded{i}") for i in range(2)]
        s_w = sem("w_rows_formed")
        s_wv = sem("w_rows_evacuated")
        s_wst = [sem(f"w_stored{i}") for i in range(2)]
        s_wl = sem("w_loaded")
        s_wh = sem("w_hi")
        s_wlo = sem("w_lo")
        s_bn = sem("tile_moments")
        s_ag = sem("tile_mean_and_variance")
        s_rs = sem("pair_rstd")
        s_ebn = sem("edge_moments")
        s_eag = sem("edge_mean_and_variance")
        s_ers = sem("edge_rstd")
        s_ri = sem("record_in_ring")
        s_dup = sem("repeats_counted")
        s_qbn = sem("group_moments")
        s_qag = sem("group_mean_and_variance")
        s_qrs = sem("group_rstd")
        s_rt = sem("router_step")
        s_stw = sem("expert_weights_loaded")
        s_ewh = sem("expert_weights_hi")
        s_ewl = sem("expert_weights_lo")
        s_sm2 = sem("moe_small_loaded")
        s_qs = sem("moe_small_made")
        s_zin = [sem(f"z_loaded{i}") for i in range(4)]
        s_xr = [sem(f"x_loaded{i}") for i in range(2)]
        s_zx = sem("z_plus_x")
        s_qst = sem("group_stats")
        s_qn = sem("group_normalised")
        s_qtp = sem("group_transposed")
        s_qth = sem("group_hi")
        s_qtl = sem("group_lo")
        s_up = sem("up_done")
        s_ge = sem("gelu_done")
        s_bc = sem("weight_spread")
        s_gs = sem("weighted")
        s_gh = sem("hidden_hi")
        s_gl = sem("hidden_lo")
        s_lg = sem("logits_done")
        s_l2 = sem("logits_shifted")
        s_ex = sem("exp_done")
        s_cw3 = sem("weights_known")
        s_cwt = sem("weights_transposed")
        s_ct = sem("weights_ready")
        s_dn = sem("down_done")
        s_oe = sem("out_written")
        s_ost = [sem(f"out_stored{i}") for i in range(4)]

        def wait_apart(eng, sem, value):
            wait(eng, sem, value)
            if not isinstance(value, int):
                eng.sem_inc(s_apart[0 if eng.engine == mybir.EngineType.DVE else 1], 1)

        def phase_of(S):
            for name, first, count in ((SA, A0, NT), (SB, B0, ET), (SC, C0, NT), (SD, D0, ET)):
                if first <= S < first + count:
                    return name, S - first
            return None, 0

        START = {SA: A0, SB: B0, SC: C0, SD: D0}
        NODES_BEFORE = {SA: 0, SC: NT}
        EDGES_BEFORE = {SB: 0, SD: ET}
        LAYER = {SA: 0, SB: 0, SC: 1, SD: 1}

        class Step:

            def __init__(self, phase, t):
                self.phase, self.t = phase, t
                self.node = phase in (SA, SC)
                self.layer = LAYER[phase]
                self.T = t + START[phase]
                if self.node:
                    self.n = t + NODES_BEFORE[phase]
                    self.g = t.div(2)
                    self.gg = t.div(2) + (NG + 1) * self.layer
                else:
                    self.e = t + EDGES_BEFORE[phase]

        def later(st, ahead):
            if st.t.i is not None:
                return Step(st.phase, st.t + ahead)
            name, k = phase_of(st.T.k + ahead)
            return None if name is None else Step(name, Pos(k))

        def walk(eng, step):
            for phase, count, unroll in ((SA, NT, 8), (SB, ET, 4), (SC, NT, 8), (SD, ET, 4)):
                stop = 2 * CS - 8 if unroll == 8 else (count - 6) // unroll * unroll
                for t in range(unroll):
                    step(Step(phase, Pos(t)))
                with eng.Fori(1, stop // unroll) as i:
                    for k in range(unroll):
                        step(Step(phase, Pos(k, i, unroll)))
                for t in range(stop, count):
                    step(Step(phase, Pos(t)))

        def w_step(st):
            if not st.node or st.t.mod(2) == 0 or (st.t.i is None and st.t.k >= 2 * CS):
                return None
            return st.t.div(2) + CS * st.layer

        def pair_rows(table, g, tiles):
            if tiles == 1:
                return table[TAIL:N, :].rearrange("(p j) d -> p j d", j=1)
            pairs = table[0:2 * P * NG, :].rearrange("(g p j) d -> g p j d", p=P, j=2)
            if g.i is None:
                return pairs[g.k]
            return pairs[bass.ds(g.times(1), 1)].rearrange("g p j d -> p (g j) d")

        def is_tail(st):
            return st.t.i is None and st.t.k == NT - 1

        def walk_groups(eng, group):
            for q in range(4):
                group(Pos(q))
            with eng.Fori(1, NQ // 4 - 1) as i:
                for k in range(4):
                    group(Pos(k, i, 4))
            for q in range(NQ - 4, NQ):
                group(Pos(q))

        def tiles_of(q):
            return QLAST if q.i is None and q.k == NQ - 1 else QT

        def missing(q):
            return q.i is None and q.k >= NQ

        block = ctx.enter_context(nc.Block())

        @block.sync
        def _(sp):
            def load_pair(phase, g):
                gg = g + (NG + 1) * LAYER[phase]
                tiles = 1 if g.i is None and g.k == NG else 2
                table = x if phase == SA else y1
                sp.dma_start(xin[:, gg.mod(4), 0:tiles, :], pair_rows(table, g, tiles)).then_inc(s_xin[gg.mod(4)], 16)

            def load_basis(layer, c):
                rows = basis[layer].rearrange("b (s i) o -> (b s) i o", s=ISUB)
                sl = slice(4 * c.k, 4 * c.k + 4) if c.i is None else bass.ds(c.times(4), 4)
                cg = c + CS * layer
                sp.dma_start(basis_t[:, cg.mod(2), :, :], rows[:, sl, :]).then_inc(s_bin[cg.mod(2)], 16)

            def store_w(layer, u):
                ug = u + CS // 2 * layer
                wait(sp, s_wv, ug.times(2, 2))
                rows = w_dram[layer].rearrange("m (u c j) o -> u j m c o", c=2, j=4)
                for j in range(4):
                    if u.i is None:
                        dst_rows = rows[u.k, j]
                    else:
                        dst_rows = rows[bass.ds(u.times(1), 1), j].rearrange("u m c o -> m (u c) o")
                    sp.dma_start(dst_rows, wevac[32 * j:32 * j + R * ISUB, ug.mod(2), :, :]).then_inc(s_wst[ug.mod(2)], 16)

            def step(st):
                if not st.node:
                    if st.phase == SB and st.t.i is None and st.t.k == 0:
                        flush_stores(SA)
                    if st.phase == SD and st.t.i is None and st.t.k == 0:
                        flush_stores(SC)
                        load_experts()
                    return
                if st.phase == SC and st.t.i is None and st.t.k == 0:
                    sp.wait_ge(s_scat, 16 * ET)
                    sp.wait_ge(s_norm, NT)
                    for g in range(4):
                        load_pair(SC, Pos(g))
                j = st.t.mod(2)
                c = w_step(st)
                if c is not None:
                    if st.t.i is not None or st.t.k < 2 * CS - 4:
                        wait(sp, s_w, c.times(1, 1))
                        load_basis(st.layer, st.t.div(2) + 2)
                    if st.t.mod(4) == 3:
                        store_w(st.layer, st.t.div(4))
                if st.t.i is None and st.t.k == 2 * CS + 1:
                    for i in range(2):
                        sp.wait_ge(s_wst[i], 64 * (CS // 4) * (st.layer + 1))
                    if st.layer:
                        sp.wait_ge(s_mm, C0)
                    sp.dma_start(wrl[:, :, :].bitcast(F32), w_dram[st.layer].rearrange("m i o -> i m o")).then_inc(s_wl, 16)
                if j == 1:
                    more = st.t.i is not None or st.g.k + 4 <= NG
                    if more:
                        if st.phase == SA:
                            wait(sp, s_norm, st.n.times(1, 1))
                        else:
                            wait(sp, s_tp, st.T.times(1, 1))
                        load_pair(st.phase, st.g + 4)
                    if st.t.i is not None or st.t.k > 1:
                        store_pair(st.phase, st.g + (-1))

            def store_pair(phase, g):
                gg = g + (NG + 1) * LAYER[phase]
                tiles = 1 if g.i is None and g.k == NG else 2
                n = g.times(2, tiles + NODES_BEFORE[phase])
                wait(sp, s_y, n)
                if tiles == 1:
                    before_gg = gg + (-1)
                    sp.wait_ge(s_ystore[before_gg.mod(2)], 16 * (before_gg.k // 2 + 1))
                table = y1 if phase == SA else z
                sp.dma_start(pair_rows(table, g, tiles), yout[:, gg.mod(2), 0:tiles, :]).then_inc(s_ystore[gg.mod(2)], 16)

            def flush_stores(phase):
                for g in range(NG - 1 if NT % 2 else NG, NG + 1):
                    store_pair(phase, Pos(g))

            def load_experts():
                sp.wait_ge(s_mm, D0)
                sp.wait_ge(s_ystore[0], 16 * (NG + 1))
                sp.wait_ge(s_ystore[1], 16 * (NG + 1))
                sp.dma_start(stage_w1[:], w1T.rearrange("(k p) f -> p k f", p=P)).then_inc(s_stw, 16)
                sp.dma_start(stage_w2[:], w2T.rearrange("(c p) d -> p c d", p=P)).then_inc(s_stw, 16)

            for t, a in ((e_type, etype), (e_src, src), (e_dst, dst)):
                sp.dma_start(t[:], a.rearrange("(p c) -> p c", p=ER)).then_inc(s_edges, 16)
            load_pair(SA, Pos(0))
            sp.dma_start(stage0[:], root[0].rearrange("(k p) o -> p k o", p=P)).then_inc(s_root[0], 16)
            for l in range(2):
                sp.dma_start(bias_b[l][:], bias[l].rearrange("(a d) -> a d", a=1).to_broadcast([P, H])).then_inc(s_small, 16)
                for s in range(R):
                    sp.dma_start(gatew[l][:, s, :], gate_w[l][s].rearrange("d a -> a d").to_broadcast([P, H])).then_inc(s_small, 16)
            for g in range(1, 4):
                load_pair(SA, Pos(g))
            for c in range(2):
                load_basis(0, Pos(c))
            sp.dma_start(stage1[:], root[1].rearrange("(k p) o -> p k o", p=P)).then_inc(s_root[1], 16)
            sp.wait_ge(s_const, 1)
            sp.dma_start(records.rearrange("(p t) c -> p t c", p=P), fill_rec[:]).then_inc(s_fill, 16)
            sp.dma_start(y1[N:N + P, :], zeros[:]).then_inc(s_zero_rows, 16)
            sp.dma_start(z[N:N + P, :], zeros[:]).then_inc(s_zero_rows, 16)
            sp.dma_start(gw[:], moe_gate_wT.rearrange("(k p) e -> p k e", p=P)).then_inc(s_sm2, 16)
            sp.dma_start(gbias[:], moe_gate_b.rearrange("(a e) -> a e", a=1).to_broadcast([P, NE])).then_inc(s_sm2, 16)
            sp.dma_start(b1[:, 0:1], sb1.rearrange("n (f a) -> (n f) a", a=1)).then_inc(s_sm2, 16)
            for c in range(1, FC):
                sp.dma_start(b1[:, c:c + 1], rb1[2 * c - 2:2 * c, :].rearrange("e (f a) -> (e f) a", a=1)).then_inc(s_sm2, 16)
            for i in range(3):
                sp.dma_start(b2[i * NR2:i * NR2 + NE, :], rb2).then_inc(s_sm2, 16)
                sp.dma_start(b2[i * NR2 + NE:(i + 1) * NR2, :], sb2).then_inc(s_sm2, 16)

            def walk_sp(st):
                if st.phase == SC and st.t.i is None and st.t.k == 0:
                    for c in range(2):
                        load_basis(1, Pos(c))
                step(st)

            walk(sp, walk_sp)

            def q_rows(table, q):
                if q.i is None and q.k == NQ - 1:
                    return table[N - QLAST * P:N, :].rearrange("(p j) d -> p j d", j=QLAST)
                groups = table[0:QT * P * (NQ - 1), :].rearrange("(q p j) d -> q p j d", p=P, j=QT)
                if q.i is None:
                    return groups[q.k]
                return groups[bass.ds(q.times(1), 1)].rearrange("q p j d -> p (q j) d")

            def q_tiles(q):
                return QLAST if q.i is None and q.k == NQ - 1 else QT

            def load_group(q):
                if q.i is None and q.k >= NQ:
                    return
                n = q_tiles(q)
                wait(sp, s_ost[q.mod(4)], q.div(4).times(16))
                sp.dma_start(zr[:, q.mod(4), 0:n, :], q_rows(z, q)).then_inc(s_zin[q.mod(4)], 16)
                wait(sp, s_zx, q.times(1, -1))
                sp.dma_start(xr[:, q.mod(2), 0:n, :], q_rows(x, q)).then_inc(s_xr[q.mod(2)], 16)

            def store_group(q):
                n = q_tiles(q)
                wait(sp, s_oe, q.times(QT, n))
                if n != QT:
                    sp.wait_ge(s_ost[(q.k - 1) % 4], 16 * ((q.k - 1) // 4 + 1))
                sp.dma_start(q_rows(out, q), zr[:, q.mod(4), 0:n, :]).then_inc(s_ost[q.mod(4)], 16)

            sp.wait_ge(s_scat, 32 * ET)
            for q in range(3):
                load_group(Pos(q))

            def group(q):
                if q.i is not None or q.k > 0:
                    store_group(q + (-1))
                load_group(q + 3)

            walk_groups(sp, group)
            store_group(Pos(NQ - 1))
            for i in range(4):
                sp.wait_ge(s_ost[i], 16 * (NQ // 4))

        @block.gpsimd
        def _(pool):
            pool.memset(ident[:], 0.0).then_inc(s_pool, 1)
            pool.memset(ones[:], 1.0).then_inc(s_pool, 1)
            pool.memset(zeros[:], 0.0).then_inc(s_pool, 1)
            pool.memset(fill_rec[:], 0).then_inc(s_pool, 1)
            pool.iota(e_iota[:], [[1, EC]], base=0, channel_multiplier=EC,
                      allow_small_or_imprecise_dtypes=True).then_inc(s_pool, 1)
            pool.iota(t_iota[:], [[1, ET + 1]], base=0, channel_multiplier=0,
                      allow_small_or_imprecise_dtypes=True).then_inc(s_pool, 1)
            pool.iota(trash_f[:], [[0, 1]], base=TRASH, channel_multiplier=1,
                      allow_small_or_imprecise_dtypes=True).then_inc(s_pool, 1)
            pool.memset(lo_row[:], 1.0).then_inc(s_pool, 1)
            pool.memset(minus_half[:], -0.5)
            pool.memset(b2lo[:], 0.0).then_inc(s_pool, 1)
            pool.wait_ge(s_pool, 9)
            pool.affine_select(out=ident[:], in_=ident[:], compare_op=ALU.not_equal, fill=1.0, base=0,
                               pattern=[[-1, P]], channel_multiplier=1).then_inc(s_pool, 1)
            pool.affine_select(out=lower[:], in_=ones[:], compare_op=ALU.is_gt, fill=0.0, base=0,
                               pattern=[[-1, P]], channel_multiplier=1).then_inc(s_pool, 1)
            pool.affine_select(out=before[:], in_=ones[:], compare_op=ALU.is_gt, fill=0.0, base=0,
                               pattern=[[1, P]], channel_multiplier=-1).then_inc(s_pool, 1)
            pool.iota(fill_rec[:, :, 0], [[0, ET]], base=TRASH, channel_multiplier=1).then_inc(s_pool, 1)
            pool.affine_select(out=lo_row[:], in_=lo_row[:], compare_op=ALU.is_ge, fill=0.0, base=-NR2,
                               pattern=[[0, 1]], channel_multiplier=1).then_inc(s_pool, 1)
            pool.wait_ge(s_pool, 14)
            pool.affine_select(out=lo_row[:], in_=lo_row[:], compare_op=ALU.is_ge, fill=0.0, base=2 * NR2 - 1,
                               pattern=[[0, 1]], channel_multiplier=-1).then_inc(s_pool, 1)
            picks = b2lo[:, :].rearrange("p (e f) -> p e f", f=64)
            pool.affine_select(out=picks, in_=picks, compare_op=ALU.not_equal, fill=1.0, base=0,
                               pattern=[[-1, NE], [0, 64]], channel_multiplier=1).then_inc(s_pool, 1)
            pool.wait_ge(s_pool, 16)
            pool.affine_select(out=picks, in_=picks, compare_op=ALU.not_equal, fill=1.0, base=-2 * NR2,
                               pattern=[[-1, NE], [0, 64]], channel_multiplier=1).then_inc(s_pool, 1)
            pool.wait_ge(s_pool, 17)
            pool.tensor_copy(sel[:], picks).then_inc(s_pool, 1)
            pool.wait_ge(s_pool, 18)
            pool.sem_inc(s_const, 1)
            for l in range(2):
                for r in range(R):
                    pool.dma_start(att_c[:, l, r:r + 1],
                                   att[l][r].rearrange("(b a) -> b a", a=1).to_broadcast([NB, ISUB])
                                   .rearrange("b (s a) -> b s a", a=1)).then_inc(s_recl, 16)

            def rstd_of(r, m, mean, var, key, index, done):
                n = r.shape[-1]
                pool.tensor_scalar(r, var, EPS, None, ALU.add).then_inc(key, 1)
                wait(pool, key, index.times(2, 1))
                pool.tensor_tensor(r, r, minus_half[:, 0:n], ALU.pow).then_inc(key, 1)
                wait_apart(pool, key, index.times(2, 2))
                for i in range(n):
                    ins = pool.tensor_scalar(m[:, i:i + 1], mean[:, i:i + 1], r[:, i:i + 1], -1.0, ALU.mult, ALU.mult)
                ins.then_inc(done, 1)

            def pair_rstd(g):
                s, n = g.mod(4), 1 if g.i is None and g.k == NG else 2
                wait_apart(pool, s_ag, g.times(2, n))
                rstd_of(rstd[:, s, 0:n], nmr[:, s, 0:n], mv[:, s, 0:n, 0], mv[:, s, 0:n, 1], s_rs,
                        g, s_stat)

            for g in range(4):
                pair_rstd(Pos(g))
            pool.wait_ge(s_fill, 16)
            pool.wait_ge(s_pos, 1)

            def records_and_rstd(i):
                for k in range(4):
                    pair_rstd(Pos(k + 4, i, 4))
                    for c in (Pos(2 * k, i, 8), Pos(2 * k + 1, i, 8)):
                        s, sl = c.mod(2), slice(c.k, c.k + 1) if i is None else bass.ds(c.times(1), 1)
                        wait(pool, s_rec, c.times(16))
                        pool.tensor_copy(r_pos[:, s:s + 1], e_pos[:, sl])
                        pool.tensor_copy(r_rec[:, s, :], e_rec[:, sl, :].rearrange("p c a -> p (c a)")).then_inc(s_ri, 1)
                        wait_apart(pool, s_ri, c.times(1, 1))
                        pool.indirect_dma_start(out=records, in_=r_rec[:, s, :], in_offset=None,
                                                out_offset=bass.IndirectOffsetOnAxis(ap=r_pos[:, s:s + 1], axis=0))\
                            .then_inc(s_rec, 16)

            records_and_rstd(None)
            with pool.Fori(1, EC // 8) as i:
                records_and_rstd(i)
            pairs_done = 4 + EC // 8 * 4
            pair_rstd(Pos(pairs_done))
            pool.wait_ge(s_rec, 16 * EC)
            rec = fill_rec
            pool.dma_start(rec[:], records.rearrange("(p t) c -> p t c", p=P)).then_inc(s_recl, 16)
            pair_rstd(Pos(pairs_done + 1))
            pool.wait_ge(s_recl, 16 * (2 * R + 1))
            pool.tensor_copy(src_slot[:], rec[:, :, 0]).then_inc(s_slots, 1)
            pool.tensor_copy(dst_slot[:], rec[:, :, 1]).then_inc(s_slots, 1)
            pool.wait_ge(s_slots, 2)
            with nc.allow_non_contiguous_dma(reason="5248 words, once"):
                pool.dma_start(src_rows.rearrange("t p -> p t"), src_slot[:]).then_inc(s_srow, 16)
            for g in range(pairs_done + 2, pairs_done + 4):
                pair_rstd(Pos(g))
            pool.wait_ge(s_srow, 16)
            pool.wait_ge(s_rooth, 2)
            pool.wait_ge(s_rootl, 2)
            pool.dma_start(same[:, :, :].bitcast(F32).rearrange("p t i -> p (t i)"),
                           src_rows.rearrange("(a t) p -> a (t p)", a=1).to_broadcast([P, ET * P])).then_inc(s_srcb, 16)

            def gather(st):
                e = st.e
                wait(pool, s_xn, e.times(1, -3))
                sl = slice(st.t.k, st.t.k + 1) if st.t.i is None else bass.ds(st.t.times(1), 1)
                pool.tensor_copy(gidx[:, e.mod(4):e.mod(4) + 1], dst_slot[:, sl]).then_inc(s_gi, 1)
                wait_apart(pool, s_gi, e.times(1, 1))
                pool.indirect_dma_start(out=gx[:, e.mod(4), :], out_offset=None, in_=x if st.phase == SB else y1,
                                        in_offset=bass.IndirectOffsetOnAxis(ap=gidx[:, e.mod(4):e.mod(4) + 1], axis=0))\
                    .then_inc(s_gx[e.mod(4)], 16)

            def scatter(st):
                e = st.e
                wait(pool, s_scat, e.times(16))
                sl = slice(st.t.k, st.t.k + 1) if st.t.i is None else bass.ds(st.t.times(1), 1)
                pool.tensor_copy(sidx[:, e.mod(2):e.mod(2) + 1], scat_slot[:, sl]).then_inc(s_si, 1)
                wait(pool, s_msg, e.times(1, 1))
                wait_apart(pool, s_si, e.times(1, 1))
                pool.indirect_dma_start(out=y1 if st.phase == SB else z,
                                        out_offset=bass.IndirectOffsetOnAxis(ap=sidx[:, e.mod(2):e.mod(2) + 1], axis=0),
                                        in_=msg[:, e.mod(2), :], in_offset=None, compute_op=ALU.add)\
                    .then_inc(s_scat, 16)

            def edge_rstd(st):
                s = st.e.mod(4)
                wait_apart(pool, s_eag, st.e.times(1, 1))
                rstd_of(erstd[:, s, :], enmr[:, s, :], emv[:, s, 0:1], emv[:, s, 1:2], s_ers,
                        st.e, s_est)

            def edges(phase):
                def one(t):
                    if t.i is not None or 0 <= t.k + 9 < ET:
                        gather(Step(phase, t + 9))
                    if phase == SB and (t.i is not None or 0 <= t.k + 6 < ET):
                        edge_rstd(Step(phase, t + 6))
                    if t.i is None and t.k < 0:
                        return
                    if t.i is None and t.k == 0:
                        if phase == SB:
                            pool.wait_ge(s_sidx, 1)
                            pool.wait_ge(s_zero_rows, 32)
                        for i in range(2):
                            pool.wait_ge(s_ystore[i], 16 * (NG + 1) // 2 * (LAYER[phase] + 1))
                    scatter(Step(phase, t))

                if phase == SD:
                    pool.wait_ge(s_scat, 16 * ET)
                for t in range(-9, 4):
                    one(Pos(t))
                with pool.Fori(1, (ET - 9) // 4) as i:
                    for k in range(4):
                        one(Pos(k, i, 4))
                for t in range((ET - 9) // 4 * 4, ET):
                    one(Pos(t))

            for g in range(pairs_done + 4, NG + 1):
                pair_rstd(Pos(g))
            edges(SB)
            edges(SD)
            pool.wait_ge(s_scat, 32 * ET)

            def group(q):
                if not missing(q + 3):
                    add_x(q + 3)
                if not missing(q + 2):
                    group_rstd(q + 2)

            def group_rstd(q):
                s, n = q.mod(2), tiles_of(q)
                wait_apart(pool, s_qag, q.times(QT, n))
                rstd_of(qrstd[:, s, 0:n], qnmr[:, s, 0:n], qmv[:, s, 0:n, 0], qmv[:, s, 0:n, 1], s_qrs,
                        q, s_qst)

            def add_x(q):
                n = tiles_of(q)
                wait(pool, s_zin[q.mod(4)], q.div(4).times(16, 16))
                wait(pool, s_xr[q.mod(2)], q.div(2).times(16, 16))
                zq = zr[:, q.mod(4), 0:n, :]
                pool.tensor_tensor(zq, zq, xr[:, q.mod(2), 0:n, :], ALU.add).then_inc(s_zx, 1)

            for q in range(3):
                add_x(Pos(q))
                if q < 2:
                    group_rstd(Pos(q))
            walk_groups(pool, group)

        @block.scalar
        def _(act):
            act.wait_ge(s_root[0], 16)
            act.activation(root1h[:], stage0[:], ACT.Copy).then_inc(s_rooth, 1)

            def norm(st):
                par, j = st.gg.mod(4), st.t.mod(2)
                wait(act, s_stat, st.gg.times(1, 1))
                wait(act, s_tp, st.T.times(1, -1))
                act.activation(xn_a[:, st.t.mod(2), :], xin[:, par, j, :], ACT.Identity,
                               bias=nmr[:, par, j:j + 1], scale=rstd[:, par, j:j + 1]).then_inc(s_norm, 1)

            def hi(st):
                wait(act, s_tp, st.T.times(1, 1))
                wait(act, s_mm, st.T.times(1, -1))
                s = st.T.mod(2)
                f = ACT.Relu if st.phase == SC else ACT.Copy
                act.activation(th[:, s, :], tpb[s][:], f).then_inc(s_hi, 1)

            def edge_xn(st):
                s = st.e.mod(4)
                wait(act, s_el, st.e.times(1, -3))
                if st.phase == SB:
                    wait(act, s_est, st.e.times(1, 1))
                    act.activation(xn_e[:, s, :], gx[:, s, :], ACT.Identity, bias=enmr[:, s, :],
                                   scale=erstd[:, s, :]).then_inc(s_xn, 1)
                else:
                    wait(act, s_gx[s], st.e.div(4).times(16, 16))
                    act.activation(xn_e[:, s, :], gx[:, s, :], ACT.Relu).then_inc(s_xn, 1)

            def edge_gated(st):
                s, s2 = st.e.mod(4), st.e.mod(2)
                wait(act, s_gate, st.e.times(1, 1))
                act.activation(gate[:, s:s + 1], logit[:, s:s + 1], ACT.Sigmoid).then_inc(s_sig, 1)
                wait(act, s_sig, st.e.times(1, 1))
                wait(act, s_tp, st.T.times(1, -1))
                act.activation(eh[:, s2, :], xn_e[:, s, :], ACT.Copy, scale=gate[:, s:s + 1]).then_inc(s_eh, 1)

            def message(st):
                wait(act, s_mm, st.T.times(1, 1))
                wait(act, s_scat, st.e.times(16, -16))
                act.activation(msg[:, st.e.mod(2), :], outb[st.T.mod(2)][:], ACT.Copy).then_inc(s_msg, 1)

            def w_evac(c):
                u = c.div(2)
                wait(act, s_w, c.times(1, 1))
                if c.mod(2) == 0:
                    wait(act, s_wst[u.mod(2)], u.div(2).times(64))
                act.activation(wevac[:, u.mod(2), c.mod(2), :], wb[c.mod(2)][:], ACT.Copy).then_inc(s_wv, 1)

            def w_hi(layer, m):
                act.wait_ge(s_wl, 16 * (layer + 1))
                act.activation(wrh[:, m, :], wrl[:, m, :].bitcast(F32), ACT.Copy).then_inc(s_wh, 1)

            def expert_hi(n):
                act.wait_ge(s_stw, 32)
                if n < FC:
                    o, i = w1h[:].rearrange("p k f -> p (k f)"), stage_w1[:].rearrange("p k f -> p (k f)")
                else:
                    o, i = w2h[:].rearrange("p k f -> p (k f)"), stage_w2[:].rearrange("p k f -> p (k f)")
                m = n % FC
                act.activation(o[:, 512 * m:512 * m + 512], i[:, 512 * m:512 * m + 512], ACT.Copy).then_inc(s_ewh, 1)

            def step(st):
                a1, a2, a4, b1_ = later(st, 1), later(st, 2), later(st, 4), later(st, -1)
                into_c = a1 and a1.phase == SC and st.phase == SB
                if into_c:
                    message(b1_)
                    message(st)
                if a1:
                    hi(a1)
                if a2 and not a2.node:
                    edge_gated(a2)
                if b1_ and not b1_.node and not into_c and not (b1_.phase == SB and st.node):
                    message(b1_)
                c = w_step(st)
                if c is not None:
                    w_evac(c)
                if a2 and a2.phase == SA:
                    norm(a2)
                if a4 and not a4.node:
                    edge_xn(a4)
                if st.t.i is None:
                    if st.phase == SA and st.t.k == 1:
                        act.wait_ge(s_root[1], 16)
                        act.activation(root2h[:], stage1[:], ACT.Copy).then_inc(s_rooth, 1)
                    if st.node and 70 <= st.t.k < 78:
                        w_hi(st.layer, st.t.k - 70)
                    if st.phase == SD and 36 <= st.t.k:
                        expert_hi(2 * (st.t.k - 36))
                        expert_hi(2 * (st.t.k - 36) + 1)

            norm(Step(SA, Pos(0)))
            norm(Step(SA, Pos(1)))
            hi(Step(SA, Pos(0)))
            walk(act, step)
            message(Step(SD, Pos(ET - 1)))

            act.wait_ge(s_scat, 32 * ET)

            def q_norm(q):
                n = tiles_of(q)
                wait(act, s_qst, q.times(1, 1))
                wait(act, s_qtp, q.times(KC))
                for j in range(n):
                    act.activation(tn[:, j, :], zr[:, q.mod(4), j, :], ACT.Identity,
                                   bias=qnmr[:, q.mod(2), j:j + 1],
                                   scale=qrstd[:, q.mod(2), j:j + 1]).then_inc(s_qn, 1)

            def q_hi(q, k):
                n = tiles_of(q)
                wait(act, s_qtp, q.times(KC, k + 1))
                if k == 0:
                    wait(act, s_dn, q.times(QT, -QT))
                act.activation(tth[:, q.mod(2), k, 0:n * P], tpb[k % 2][:, 0:n * P], ACT.Copy).then_inc(s_qth, 1)

            def gelu(q, c):
                n = tiles_of(q) * P
                u = 5 * q.k + c
                wait(act, s_up, q.times(FC, c + 1))
                wait(act, s_gl, q.times(FC, c - 1))
                act.activation(gel[:, u % 2, 0:n], outb[u % 2][:, 0:n], ACT.Gelu,
                               bias=b1[:, c:c + 1]).then_inc(s_ge, 1)

            def g_hi(q, c):
                n = tiles_of(q) * P
                if c == 0:
                    wait(act, s_ge, q.times(FC, 1))
                    wait(act, s_dn, q.times(QT))
                    source = gel[:, (5 * q.k) % 2, 0:n]
                else:
                    wait(act, s_gs, q.times(NE // 2, c))
                    source = gsc[:, (c - 1) % 2, 0:n]
                act.activation(gth[:, c, 0:n], source, ACT.Copy).then_inc(s_gh, 1)

            def q_exp(q):
                n = tiles_of(q)
                wait(act, s_l2, q.times(1, 1))
                act.activation(ex[:, 0:n, :], lg2[:, 0:n, :], ACT.Exp).then_inc(s_ex, 1)

            def q_weights(q):
                n = tiles_of(q) * P
                wait(act, s_cwt, q.times(1, 1))
                act.activation(cwt[:, q.mod(2), 0:n], bank[7][0:3 * NR2, 0:n], ACT.Copy).then_inc(s_ct, 1)

            def group(q):
                nxt = q + 1
                for c in range(FC):
                    gelu(q, c)
                    if c == 0:
                        g_hi(q, c)
                    if c < KC and not missing(nxt):
                        q_hi(nxt, c)
                    if c:
                        g_hi(q, c)
                if not missing(q + 2):
                    q_norm(q + 2)
                if not missing(nxt):
                    q_exp(nxt)
                    q_weights(nxt)

            q_norm(Pos(0))
            for k in range(KC):
                q_hi(Pos(0), k)
            q_exp(Pos(0))
            q_norm(Pos(1))
            q_weights(Pos(0))
            walk_groups(act, group)

        @block.tensor
        def _(pe):
            def product(out_ap, hi_t, lo_t, hi_m, lo_m, ks, start=True, stop=True):
                ks = list(ks)
                for k in ks:
                    for a, b in ((hi_t, hi_m), (lo_t, hi_m), (hi_t, lo_m)):
                        first = start and k == ks[0] and a is hi_t and b is hi_m
                        last = stop and k == ks[-1] and b is lo_m
                        ins = pe.matmul(out_ap, a(k), b(k), start=first, stop=last)
                return ins

            pe.wait_ge(s_const, 1)
            pe.wait_ge(s_cnt, 1)
            pe.matmul(cnt[0:ER, 0:1], before[0:ER, 0:ER], e_scan[:, EC - 1:EC], start=True, stop=True)
            pe.matmul(cnt[:, 1:2], ones[0:ER, :], e_scan[:, EC - 1:EC], start=True, stop=True).then_inc(s_cnt, 1)

            def transpose(st):
                s = st.T.mod(2)
                wait(pe, s_lo, st.T.times(1, -1))
                if st.node:
                    if st.phase == SA:
                        wait(pe, s_norm, st.n.times(1, 1))
                        source = xn_a[:, st.t.mod(2), :]
                    else:
                        if st.t.mod(2) == 0:
                            wait(pe, s_xin[st.gg.mod(4)], st.gg.div(4).times(16, 16))
                        source = xin[:, st.gg.mod(4), st.t.mod(2), :]
                    for k in range(KC):
                        ins = pe.transpose(tpb[s][:, k * P:(k + 1) * P], source[:, k * P:(k + 1) * P], ident[:])
                    ins.then_inc(s_tp, 1)
                else:
                    if st.phase == SB and st.t.i is None and st.t.k == 0:
                        pe.wait_ge(s_same, ET)
                    wait(pe, s_el, st.e.times(1, 1))
                    s2 = st.e.mod(2)
                    m = same[:, st.t.k, :] if st.t.i is None else same[:, bass.ds(st.t.times(1), 1), :].rearrange("p t i -> p (t i)")
                    for k in range(KC):
                        pe.matmul(tpb[s][:, k * P:(k + 1) * P], eh[:, s2, k * P:(k + 1) * P], m, start=True, stop=False)
                        ins = pe.matmul(tpb[s][:, k * P:(k + 1) * P], el[:, s2, k * P:(k + 1) * P], m, start=False, stop=True)
                    ins.then_inc(s_tp, 1)

            def multiply(st):
                s = st.T.mod(2)
                wait(pe, s_lo, st.T.times(1, 1))
                before2 = later(st, -2)
                if before2:
                    if before2.node:
                        wait(pe, s_y, before2.n.times(1, 1))
                    else:
                        wait(pe, s_msg, before2.e.times(1, 1))
                if st.node:
                    rh, rl = (root1h, root1l) if st.layer == 0 else (root2h, root2l)
                    ins = product(outb[s][:], lambda k: th[:, s, k * P:(k + 1) * P], lambda k: tl[:, s, k * P:(k + 1) * P],
                                  lambda k: rh[:, k, :], lambda k: rl[:, k, :], range(KC))
                else:
                    sl = slice(st.t.k, st.t.k + 1) if st.t.i is None else bass.ds(st.t.times(1), 1)
                    r = pe.value_load(rel[0:1, sl], min_val=0, max_val=R - 1)

                    def w(t):
                        return lambda k: t[:, bass.ds(r * ISUB + k, 1), :].rearrange("p m o -> p (m o)")

                    ins = product(outb[s][:], lambda k: th[:, s, k * P:(k + 1) * P], lambda k: tl[:, s, k * P:(k + 1) * P],
                                  w(wrh), w(wrl), range(KC))
                ins.then_inc(s_mm, 1)

            def w_rows(c, layer):
                wait(pe, s_bin[c.mod(2)], c.div(2).times(16, 16))
                wait(pe, s_wv, c.times(1, -1))
                for j in range(4):
                    ins = pe.matmul(wb[c.mod(2)][32 * j:32 * j + 32, :], att_block[layer][:], basis_t[:, c.mod(2), j, :],
                                    start=True, stop=True, tile_position=(0, 32 * j))
                ins.then_inc(s_w, 1)

            def step(st):
                a1 = later(st, 1)
                into_c = a1 and a1.phase == SC and st.phase == SB
                if a1 and not into_c:
                    transpose(a1)
                if st.t.i is None and st.t.k == 0:
                    if st.phase == SA:
                        pe.wait_ge(s_rootl, 1)
                    if st.phase == SB:
                        pe.wait_ge(s_wlo, R * ISUB)
                    if st.phase == SC:
                        pe.wait_ge(s_rootl, 2)
                    if st.phase == SD:
                        pe.wait_ge(s_wlo, 2 * R * ISUB)
                multiply(st)
                if into_c:
                    transpose(a1)
                c = w_step(st)
                if c is not None:
                    w_rows(c, st.layer)

            transpose(Step(SA, Pos(0)))
            walk(pe, step)

            pe.wait_ge(s_scat, 32 * ET)
            pe.wait_ge(s_ewl, 2 * FC)
            pe.wait_ge(s_qs, 1)

            def q_transpose(q, k):
                n = tiles_of(q)
                if k == 0:
                    wait(pe, s_qn, q.times(QT, n))
                wait(pe, s_qtl, q.times(KC, k - 1))
                for j in range(n):
                    ins = pe.transpose(tpb[k % 2][:, j * P:(j + 1) * P], tn[:, j, k * P:(k + 1) * P], ident[:])
                ins.then_inc(s_qtp, 1)

            def up(q, c):
                n = tiles_of(q) * P
                u = 5 * q.k + c
                if c == 0:
                    wait(pe, s_qtl, q.times(KC, KC))
                wait(pe, s_ge, q.times(FC, c - 1))
                s = q.mod(2)
                product(outb[u % 2][:, 0:n], lambda k: w1h[:, k, c * P:(c + 1) * P], lambda k: w1l[:, k, c * P:(c + 1) * P],
                        lambda k: tth[:, s, k, 0:n], lambda k: ttl[:, s, k, 0:n], range(KC)).then_inc(s_up, 1)

            def spread(q, c):
                n = tiles_of(q) * P
                if c == 1:
                    wait(pe, s_ct, q.times(1, 1))
                wait(pe, s_gs, q.times(NE // 2, c - 1))
                pe.matmul(cnt[:, 0:n], sel[:, 2 * c - 2:2 * c, :].rearrange("p e f -> p (e f)"), cwt[:, q.mod(2), 0:n],
                          start=True, stop=True).then_inc(s_bc, 1)

            def logits(q):
                wait(pe, s_qtl, q.times(KC, KC))
                wait(pe, s_ct, q.times(1))
                n, s = tiles_of(q), q.mod(2)
                for j in range(n):
                    ins = product(bank[7][:, j * NE:(j + 1) * NE],
                                  lambda k: tth[:, s, k, j * P:(j + 1) * P], lambda k: ttl[:, s, k, j * P:(j + 1) * P],
                                  lambda k: gwh[:, k, :], lambda k: gwl[:, k, :], range(KC))
                ins.then_inc(s_lg, 1)

            def transpose_weights(q):
                wait(pe, s_cw3, q.times(1, 1))
                for j in range(tiles_of(q)):
                    ins = pe.transpose(bank[7][0:3 * NR2, j * P:(j + 1) * P],
                                       cw3[:, j, :, :].rearrange("p a b -> p (a b)"), ident[:])
                ins.then_inc(s_cwt, 1)

            def down(q, j):
                s = j % 2
                wait(pe, s_oe, q.times(QT, j - 1))
                o = wb[s][:]
                pe.matmul(o, cwt[:, q.mod(2), j * P:(j + 1) * P], b2r[:], start=True, stop=False)
                for c in range(FC):
                    if j == 0:
                        wait(pe, s_gl, q.times(FC, c + 1))
                    ins = product(o, lambda k: gth[:, k, j * P:(j + 1) * P], lambda k: gtl[:, k, j * P:(j + 1) * P],
                                  lambda k: w2h[:, k, :], lambda k: w2l[:, k, :], [c], start=False, stop=c == FC - 1)
                ins.then_inc(s_dn, 1)

            def group(q):
                nxt = q + 1
                for c in range(FC):
                    up(q, c)
                    if c:
                        spread(q, c)
                    if c < KC and not missing(nxt):
                        q_transpose(nxt, c)
                if not missing(nxt):
                    logits(nxt)
                for j in range(tiles_of(q)):
                    if j == tiles_of(q) - 1 and not missing(nxt):
                        transpose_weights(nxt)
                    down(q, j)

            for k in range(KC):
                q_transpose(Pos(0), k)
            logits(Pos(0))
            transpose_weights(Pos(0))
            walk_groups(pe, group)

        @block.vector
        def _(dve):
            chained = [0]

            def link(ins):
                chained[0] += 1
                ins.then_inc(s_chain, 1)
                dve.wait_ge(s_chain, chained[0])

            dve.wait_ge(s_edges, 48)
            dve.wait_ge(s_const, 1)
            link(dve.tensor_scalar(e_zero[:], e_type[:], 0, None, ALU.is_equal))
            dve.tensor_tensor_scan(e_scan[:], ones[0:ER, 0:EC], e_zero[:], 0.0, ALU.mult, ALU.add).then_inc(s_cnt, 1)
            dve.tensor_copy(e_rec[:, :, 0], e_src[:])
            link(dve.tensor_copy(e_rec[:, :, 1], e_dst[:]))
            dve.wait_ge(s_cnt, 2)
            dve.tensor_copy(n_colf[0:ER, 0:1], cnt[0:ER, 0:1])
            link(dve.tensor_copy(n_colf[:, 1:2], cnt[:, 1:2]))
            link(dve.tensor_copy(n_col[:, 0:1], n_colf[:, 1:2]))
            link(dve.tensor_scalar(n_col[:, 1:2], n_col[:, 0:1], P - 1, None, ALU.add))
            link(dve.tensor_scalar(n_col[:, 2:3], n_col[:, 1:2], 7, None, ALU.logical_shift_right))
            link(dve.tensor_copy(n_colf[:, 2:3], n_col[:, 2:3]))
            dve.tensor_scalar(rel[:], t_iota[:], n_colf[:, 2:3], None, ALU.is_ge)
            link(dve.tensor_scalar(n_colf[:, 3:4], n_colf[:, 2:3], float(P), None, ALU.mult))
            link(dve.tensor_tensor(e_f[:, 0, :], e_scan[:], e_zero[:], ALU.subtract))
            link(dve.tensor_scalar(e_f[:, 0, :], e_f[:, 0, :], n_colf[0:ER, 0:1], None, ALU.add))
            link(dve.tensor_tensor(e_f[:, 1, :], e_iota[:], e_f[:, 0, :], ALU.subtract))
            link(dve.tensor_scalar(e_f[:, 1, :], e_f[:, 1, :], n_colf[0:ER, 3:4], None, ALU.add))
            link(dve.tensor_tensor(e_f[:, 2, :], e_f[:, 0, :], e_f[:, 1, :], ALU.subtract))
            link(dve.tensor_tensor(e_f[:, 2, :], e_f[:, 2, :], e_zero[:], ALU.mult))
            link(dve.tensor_tensor(e_i[:, 0, :], e_f[:, 2, :], e_f[:, 1, :], ALU.add))
            dve.tensor_scalar(e_i[:, 1, :], e_i[:, 0, :], P - 1, None, ALU.bitwise_and)
            link(dve.tensor_scalar(e_i[:, 2, :], e_i[:, 0, :], 7, None, ALU.logical_shift_right))
            dve.scalar_tensor_tensor(out=e_pos[:], in0=e_i[:, 1, :], scalar=float(ET), in1=e_i[:, 2, :],
                                     op0=ALU.mult, op1=ALU.add).then_inc(s_pos, 1)

            dve.wait_ge(s_recl, 16 * 2 * R)
            link(dve.tensor_reduce(sub_mask[:], ident[0:BP, 0:BP].rearrange("p (b s) -> p s b", s=ISUB), AX_X, ALU.add))
            for l in range(2):
                link(dve.memset(att_block[l][:], 0.0))
                for r in range(R):
                    ins = dve.tensor_scalar(att_block[l][:, r * ISUB:(r + 1) * ISUB], sub_mask[:], att_c[:, l, r:r + 1],
                                            None, ALU.mult)
                link(ins)

            def pair_stats(st):
                par, j = st.gg.mod(4), st.t.mod(2)
                n = 1 if is_tail(st) else 2
                if j == 0:
                    wait(dve, s_xin[par], st.gg.div(4).times(16, 16))
                dve.bn_stats(bn[:, par, j, :], xin[:, par, j, :]).then_inc(s_bn, 1)
                if j == n - 1:
                    wait_apart(dve, s_bn, st.n.times(1, 1))
                    for i in range(n):
                        dve.bn_aggr(mv[:, par, i, :], bn[:, par, i, :]).then_inc(s_ag, 1)

            def lo(st):
                wait(dve, s_hi, st.T.times(1, 1))
                s = st.T.mod(2)
                if st.phase == SC:
                    ins = dve.scalar_tensor_tensor(out=tl[:, s, :], in0=tpb[s][:], scalar=0.0, in1=th[:, s, :].bitcast(F32),
                                                   op0=ALU.max, op1=ALU.subtract)
                else:
                    ins = dve.tensor_tensor(tl[:, s, :], tpb[s][:], th[:, s, :].bitcast(F32), ALU.subtract)
                ins.then_inc(s_lo, 1)

            def y_out(st):
                wait(dve, s_mm, st.T.times(1, 1))
                if st.t.mod(2) == 0:
                    wait(dve, s_ystore[st.gg.mod(2)], st.gg.div(2).times(16))
                if st.t.i is None and st.t.k == 0 and st.phase == SA:
                    dve.wait_ge(s_small, 16 * 2 * (R + 1))
                dve.tensor_tensor(yout[:, st.gg.mod(2), st.t.mod(2), :], outb[st.T.mod(2)][:], bias_b[st.layer][:],
                                  ALU.add).then_inc(s_y, 1)

            def edge_stats(st):
                s, e = st.e.mod(4), st.e
                wait(dve, s_gx[s], e.div(4).times(16, 16))
                wait(dve, s_xn, e.times(1, -3))
                dve.bn_stats(ebn[:, s, :], gx[:, s, :]).then_inc(s_ebn, 1)
                wait_apart(dve, s_ebn, e.times(1, 1))
                dve.bn_aggr(emv[:, s, :], ebn[:, s, :]).then_inc(s_eag, 1)

            def edge_gate(st):
                s = st.e.mod(4)
                sl = slice(st.t.k, st.t.k + 1) if st.t.i is None else bass.ds(st.t.times(1), 1)
                r = dve.value_load(rel[0:1, sl], min_val=0, max_val=R - 1)
                wait(dve, s_xn, st.e.times(1, 1))
                wait(dve, s_gate, st.e.times(1))
                dve.scalar_tensor_tensor(out=scratch[:], in0=xn_e[:, s, :], scalar=1.0,
                                         in1=gatew[st.layer][:, bass.ds(r, 1), :].rearrange("p r d -> p (r d)"),
                                         op0=ALU.mult, op1=ALU.mult, accum_out=logit[:, s:s + 1]).then_inc(s_gate, 1)

            def edge_lo(st):
                s, s2 = st.e.mod(4), st.e.mod(2)
                wait(dve, s_eh, st.e.times(1, 1))
                dve.scalar_tensor_tensor(out=el[:, s2, :], in0=xn_e[:, s, :], scalar=gate[:, s:s + 1],
                                         in1=eh[:, s2, :].bitcast(F32), op0=ALU.mult, op1=ALU.subtract).then_inc(s_el, 1)

            def w_lo(layer, m):
                dve.wait_ge(s_wh, R * ISUB * layer + m + 1)
                dve.tensor_tensor(wrl[:, m, :], wrl[:, m, :].bitcast(F32), wrh[:, m, :].bitcast(F32),
                                  ALU.subtract).then_inc(s_wlo, 1)

            def expert_lo(n):
                dve.wait_ge(s_ewh, n + 1)
                if n < FC:
                    o, i, h = w1l, stage_w1, w1h
                else:
                    o, i, h = w2l, stage_w2, w2h
                m = slice(512 * (n % FC), 512 * (n % FC) + 512)
                o, i, h = (t[:].rearrange("p k f -> p (k f)")[:, m] for t in (o, i, h))
                dve.tensor_tensor(o, i, h.bitcast(F32), ALU.subtract).then_inc(s_ewl, 1)

            def find_repeats(first, count):
                last = min(first + count, ET)
                for t in range(first, last):
                    dve.tensor_scalar(same[:, t, :], same[:, t, :].bitcast(F32), src_slot[:, t:t + 1], None,
                                      ALU.is_equal).then_inc(s_same, 1)
                dve.wait_ge(s_same, last)
                wait(dve, s_dup, first)
                for t in range(first, last):
                    dve.scalar_tensor_tensor(out=msg[:, 1, (t - first) * P:(t - first + 1) * P], in0=same[:, t, :].bitcast(F32), scalar=1.0, in1=lower[:],
                                             op0=ALU.mult, op1=ALU.mult, accum_out=dups[:, t:t + 1]).then_inc(s_dup, 1)

            def scatter_rows():
                dve.wait_ge(s_dup, ET)
                link(dve.tensor_scalar(keep[:], dups[:], 0.5, None, ALU.is_lt))
                link(dve.tensor_scalar(dups[:], src_slot[:], trash_f[:, 0:1], None, ALU.subtract))
                link(dve.tensor_tensor(dups[:], dups[:], keep[:], ALU.mult))
                dve.tensor_scalar(scat_slot[:], dups[:], trash_f[:, 0:1], None, ALU.add).then_inc(s_sidx, 1)

            def step(st):
                a1, a2, a3, a6, b1_ = (later(st, n) for n in (1, 2, 3, 6, -1))
                if a1:
                    lo(a1)
                if a2 and not a2.node:
                    edge_lo(a2)
                if b1_ and b1_.node:
                    y_out(b1_)
                if a3 and not a3.node:
                    edge_gate(a3)
                if a6 and a6.phase == SA:
                    pair_stats(a6)
                if a6 and a6.phase == SB:
                    edge_stats(a6)
                if st.t.i is None:
                    if st.phase == SA and st.t.k == 1:
                        dve.wait_ge(s_rooth, 2)
                        dve.tensor_tensor(root2l[:], stage1[:], root2h[:].bitcast(F32), ALU.subtract).then_inc(s_rootl, 1)
                    if st.phase == SA and st.t.k == 64:
                        dve.wait_ge(s_srcb, 16)
                    if st.phase == SA and 64 <= st.t.k < 78:
                        find_repeats(3 * (st.t.k - 64), 3)
                    if st.phase == SA and st.t.k == 78:
                        scatter_rows()
                    if st.node and 70 <= st.t.k < 78:
                        w_lo(st.layer, st.t.k - 70)
                    if st.phase == SD and 36 <= st.t.k:
                        expert_lo(2 * (st.t.k - 36))
                        expert_lo(2 * (st.t.k - 36) + 1)

            for t in range(2):
                pair_stats(Step(SA, Pos(t)))
            dve.wait_ge(s_rooth, 1)
            dve.tensor_tensor(root1l[:], stage0[:], root1h[:].bitcast(F32), ALU.subtract).then_inc(s_rootl, 1)
            for t in range(2, 6):
                pair_stats(Step(SA, Pos(t)))
            lo(Step(SA, Pos(0)))
            walk(dve, step)

            dve.wait_ge(s_sm2, 16 * (2 + FC + 6))
            link(dve.tensor_copy(gwh[:], gw[:]))
            dve.tensor_tensor(gwl[:], gw[:], gwh[:].bitcast(F32), ALU.subtract)
            link(dve.tensor_copy(b2r[:], b2[:]))
            link(dve.tensor_tensor(b2lo[:], b2[:], b2r[:].bitcast(F32), ALU.subtract))
            link(dve.tensor_tensor(b2lo[:], b2lo[:], b2r[:].bitcast(F32), ALU.subtract))
            dve.scalar_tensor_tensor(out=b2r[:], in0=b2lo[:], scalar=lo_row[:, 0:1], in1=b2r[:].bitcast(F32),
                                     op0=ALU.mult, op1=ALU.add).then_inc(s_chain, 1)
            chained[0] += 1
            dve.wait_ge(s_chain, chained[0])
            dve.wait_ge(s_scat, 32 * ET)
            dve.memset(topv[:], -1.0)
            dve.memset(cw3[:, :, 0:2, :], 1.0)
            dve.memset(cw3[:, :, 2, :], 0.0).then_inc(s_qs, 1)
            dve.wait_ge(s_qs, 1)

            def q_stats(q, js, done):
                s = q.mod(2)
                for j in js:
                    if j == 0:
                        wait(dve, s_zx, q.times(1, 1))
                    dve.bn_stats(qbn[:, s, j, :], zr[:, q.mod(4), j, :]).then_inc(s_qbn, 1)
                if done:
                    n = tiles_of(q)
                    wait_apart(dve, s_qbn, q.times(QT, n))
                    for j in range(n):
                        dve.bn_aggr(qmv[:, s, j, :], qbn[:, s, j, :]).then_inc(s_qag, 1)

            def q_lo(q, k):
                n, s = tiles_of(q) * P, q.mod(2)
                wait(dve, s_qth, q.times(KC, k + 1))
                dve.tensor_tensor(ttl[:, s, k, 0:n], tpb[k % 2][:, 0:n], tth[:, s, k, 0:n].bitcast(F32),
                                  ALU.subtract).then_inc(s_qtl, 1)

            def weigh(q, c):
                n = tiles_of(q) * P
                wait(dve, s_ge, q.times(FC, c + 1))
                wait(dve, s_bc, q.times(NE // 2, c))
                dve.tensor_tensor(gsc[:, (c - 1) % 2, 0:n], gel[:, (5 * q.k + c) % 2, 0:n], cnt[:, 0:n],
                                  ALU.mult).then_inc(s_gs, 1)

            def g_lo(q, c):
                n = tiles_of(q) * P
                wait(dve, s_gh, q.times(FC, c + 1))
                source = gel[:, (5 * q.k) % 2, 0:n] if c == 0 else gsc[:, (c - 1) % 2, 0:n]
                dve.tensor_tensor(gtl[:, c, 0:n], source, gth[:, c, 0:n].bitcast(F32), ALU.subtract).then_inc(s_gl, 1)

            def steps(q, total):
                done = [0]

                def chain(ins, last=False):
                    done[0] += 1
                    ins.then_inc(s_rt, 1)
                    wait_apart(dve, s_rt, q.times(total, done[0]))
                return chain, done

            ROUTER = 13

            def route_a(q, chain):
                n = tiles_of(q)
                wait(dve, s_lg, q.times(1, 1))
                chain(dve.tensor_tensor(lg[:, 0:n, :], bank[7][:, 0:n * NE].rearrange("p (j e) -> p j e", e=NE),
                                        gbias[:].rearrange("p (a e) -> p a e", a=1).to_broadcast([P, n, NE]), ALU.add))
                chain(dve.tensor_reduce(mx[:, 0:n], lg[:, 0:n, :], AX_X, ALU.max))
                wait(dve, s_ex, q.times(1))
                dve.tensor_tensor(lg2[:, 0:n, :], lg[:, 0:n, :],
                                  mx[:, 0:n].rearrange("p (j a) -> p j a", a=1).to_broadcast([P, n, NE]),
                                  ALU.subtract).then_inc(s_l2, 1)

            def route_b(q, chain):
                n = tiles_of(q)
                wait(dve, s_ex, q.times(1, 1))
                chain(dve.tensor_reduce(sm[:, 0:n], ex[:, 0:n, :], AX_X, ALU.add))
                chain(dve.reciprocal(rc[:, 0:n], sm[:, 0:n]))
                chain(dve.tensor_tensor(pr[:, 0:n, :], ex[:, 0:n, :],
                                        rc[:, 0:n].rearrange("p (j a) -> p j a", a=1).to_broadcast([P, n, NE]), ALU.mult))
                for j in range(n):
                    ins = dve.max(mx8[:, j, :], pr[:, j, :])
                chain(ins)
                chain(dve.tensor_copy(topv[:, 0:n, 0:2], mx8[:, 0:n, 0:2]))
                for j in range(n):
                    ins = dve.match_replace(rest[:, j, :], topv[:, j, :], pr[:, j, :], 0.0)
                chain(ins)
                chain(dve.tensor_tensor(cw[:, 0:n, :], pr[:, 0:n, :], rest[:, 0:n, :], ALU.subtract))
                chain(dve.tensor_copy(cwh[:, 0:n, :], cw[:, 0:n, :]))
                wait(dve, s_cwt, q.times(1))
                chain(dve.tensor_copy(cw3[:, 0:n, 0, 0:NE], cwh[:, 0:n, :].bitcast(F32)))
                chain(dve.tensor_copy(cw3[:, 0:n, 1, 0:NE], cwh[:, 0:n, :].bitcast(F32)))
                chain(dve.tensor_tensor(cw3[:, 0:n, 2, 0:NE], cw[:, 0:n, :], cwh[:, 0:n, :].bitcast(F32), ALU.subtract))
                dve.sem_inc(s_cw3, 1)

            def q_out(q, j):
                wait(dve, s_dn, q.times(QT, j + 1))
                zt = zr[:, q.mod(4), j, :]
                dve.tensor_tensor(zt, wb[j % 2][:], zt, ALU.add).then_inc(s_oe, 1)

            def group(q):
                nxt, nn = q + 1, q + 2
                for c in range(FC):
                    if c:
                        weigh(q, c)
                    else:
                        g_lo(q, c)
                    if c < KC and not missing(nxt):
                        q_lo(nxt, c)
                    if c:
                        g_lo(q, c)
                    if not missing(nn) and c < tiles_of(nn):
                        q_stats(nn, [c], c == tiles_of(nn) - 1)
                chain, _ = steps(nxt, ROUTER)
                if not missing(nxt):
                    route_a(nxt, chain)
                q_out(q, 0)
                if not missing(nxt):
                    route_b(nxt, chain)
                for j in range(1, tiles_of(q)):
                    q_out(q, j)

            q_stats(Pos(0), range(QT), True)
            for k in range(KC):
                q_lo(Pos(0), k)
            chain, _ = steps(Pos(0), ROUTER)
            route_a(Pos(0), chain)
            q_stats(Pos(1), range(QT), True)
            route_b(Pos(0), chain)
            walk_groups(dve, group)


def kernel(**inputs):
    import numpy as _np
    import concourse.bacc as _bacc
    from concourse import mybir as _mybir
    from concourse.bass_utils import run_bass_kernel_spmd as _run

    nc = _bacc.Bacc("TRN2", target_bir_lowering=False, num_devices=1)
    f = {k.replace("L0_", ""): _np.asarray(v) for k, v in inputs.items()}
    laid = {k: f[k] for k in ("x", "src", "dst", "edge_type_2", "gnn_basis1", "gnn_basis2", "gnn_att1", "gnn_att2",
                              "gnn_gate_w1", "gnn_gate_w2", "gnn_root1", "gnn_root2", "gnn_bias1", "gnn_bias2",
                              "ffn_gate_b", "ffn_sb1", "ffn_rb1", "ffn_sb2", "ffn_rb2")}
    d = f["x"].shape[1]
    laid["gate_wT"] = f["ffn_gate_w"].T
    laid["w1T"] = _np.concatenate([f["ffn_sw1"].reshape(-1, d), f["ffn_rw1"].reshape(-1, d)]).T
    laid["w2T"] = _np.concatenate([f["ffn_sw2"].transpose(0, 2, 1).reshape(-1, d),
                                   f["ffn_rw2"].transpose(0, 2, 1).reshape(-1, d)])
    arrays, ap = {}, {}
    for name, a in laid.items():
        a = _np.ascontiguousarray(a)
        arrays["in_" + name] = a
        ap[name] = nc.dram_tensor("in_" + name, a.shape, _mybir.dt.from_np(a.dtype), kind="ExternalInput").ap()
    out = nc.dram_tensor("out", f["x"].shape, _mybir.dt.from_np(f["x"].dtype), kind="ExternalOutput").ap()
    gnn_moe_kernel(nc, ap["x"], ap["src"], ap["dst"], ap["edge_type_2"], [ap["gnn_basis1"], ap["gnn_basis2"]],
                   [ap["gnn_att1"], ap["gnn_att2"]], [ap["gnn_gate_w1"], ap["gnn_gate_w2"]],
                   [ap["gnn_root1"], ap["gnn_root2"]], [ap["gnn_bias1"], ap["gnn_bias2"]],
                   ap["gate_wT"], ap["ffn_gate_b"], ap["w1T"], ap["ffn_sb1"], ap["ffn_rb1"], ap["w2T"],
                   ap["ffn_sb2"], ap["ffn_rb2"], out)
    r = _run(nc, [arrays], core_ids=[0])
    return r.results[0]["out"]
```
